# Optimizing a Trainium2 kernel written in Bass

```python
import numpy as np
import jax
import jax.numpy as jnp

def _softmax(x, axis=-1):
    return jax.nn.softmax(x, axis=axis)

def _gelu(x):
    return jax.nn.gelu(x, approximate=True)

def _silu(x):
    return jax.nn.silu(x)

def _sigmoid(x):
    return jax.nn.sigmoid(x)

def _layernorm(x, axis=-1, eps=1e-05):
    m = jnp.mean(x, axis=axis, keepdims=True)
    v = jnp.var(x, axis=axis, keepdims=True)
    return (x - m) / jnp.sqrt(v + eps)

def _scatter_add(tgt, idx, src, axis=0):
    return tgt.at[idx].add(src)

def _segment_sum(src, seg, n):
    return jax.ops.segment_sum(src, seg, n)
kernel_name = 'mk_dlrm_tower_d1_rec_r8_85b2f7'

def setup_inputs(seed: int=0):
    np.random.seed(seed)
    _w = jnp.asarray

    def _rec_inputs():
        import jax
        import jax.numpy as jnp
        _tk = jax.random.key(seed)
        ids = jnp.stack([jax.random.randint(jax.random.fold_in(_tk, 200 + f), (512,), 0, v, jnp.int32) for f, v in enumerate([1250, 1250, 125000, 1000, 1250, 12500, 1000, 1250, 12500, 12500, 1250, 1250, 12500, 1000, 1250, 12500, 1250, 1000, 12500, 1000, 1250, 1250, 12500, 1250, 1250, 1000])], axis=1)
        tbl_0 = 0.05 * jax.random.normal(jax.random.fold_in(_tk, 500 + 0), (1250, 128), jnp.float32)
        tbl_1 = 0.05 * jax.random.normal(jax.random.fold_in(_tk, 500 + 1), (1250, 128), jnp.float32)
        tbl_2 = 0.05 * jax.random.normal(jax.random.fold_in(_tk, 500 + 2), (125000, 128), jnp.float32)
        tbl_3 = 0.05 * jax.random.normal(jax.random.fold_in(_tk, 500 + 3), (1000, 128), jnp.float32)
        tbl_4 = 0.05 * jax.random.normal(jax.random.fold_in(_tk, 500 + 4), (1250, 128), jnp.float32)
        tbl_5 = 0.05 * jax.random.normal(jax.random.fold_in(_tk, 500 + 5), (12500, 128), jnp.float32)
        tbl_6 = 0.05 * jax.random.normal(jax.random.fold_in(_tk, 500 + 6), (1000, 128), jnp.float32)
        tbl_7 = 0.05 * jax.random.normal(jax.random.fold_in(_tk, 500 + 7), (1250, 128), jnp.float32)
        tbl_8 = 0.05 * jax.random.normal(jax.random.fold_in(_tk, 500 + 8), (12500, 128), jnp.float32)
        tbl_9 = 0.05 * jax.random.normal(jax.random.fold_in(_tk, 500 + 9), (12500, 128), jnp.float32)
        tbl_10 = 0.05 * jax.random.normal(jax.random.fold_in(_tk, 500 + 10), (1250, 128), jnp.float32)
        tbl_11 = 0.05 * jax.random.normal(jax.random.fold_in(_tk, 500 + 11), (1250, 128), jnp.float32)
        tbl_12 = 0.05 * jax.random.normal(jax.random.fold_in(_tk, 500 + 12), (12500, 128), jnp.float32)
        tbl_13 = 0.05 * jax.random.normal(jax.random.fold_in(_tk, 500 + 13), (1000, 128), jnp.float32)
        tbl_14 = 0.05 * jax.random.normal(jax.random.fold_in(_tk, 500 + 14), (1250, 128), jnp.float32)
        tbl_15 = 0.05 * jax.random.normal(jax.random.fold_in(_tk, 500 + 15), (12500, 128), jnp.float32)
        tbl_16 = 0.05 * jax.random.normal(jax.random.fold_in(_tk, 500 + 16), (1250, 128), jnp.float32)
        tbl_17 = 0.05 * jax.random.normal(jax.random.fold_in(_tk, 500 + 17), (1000, 128), jnp.float32)
        tbl_18 = 0.05 * jax.random.normal(jax.random.fold_in(_tk, 500 + 18), (12500, 128), jnp.float32)
        tbl_19 = 0.05 * jax.random.normal(jax.random.fold_in(_tk, 500 + 19), (1000, 128), jnp.float32)
        tbl_20 = 0.05 * jax.random.normal(jax.random.fold_in(_tk, 500 + 20), (1250, 128), jnp.float32)
        tbl_21 = 0.05 * jax.random.normal(jax.random.fold_in(_tk, 500 + 21), (1250, 128), jnp.float32)
        tbl_22 = 0.05 * jax.random.normal(jax.random.fold_in(_tk, 500 + 22), (12500, 128), jnp.float32)
        tbl_23 = 0.05 * jax.random.normal(jax.random.fold_in(_tk, 500 + 23), (1250, 128), jnp.float32)
        tbl_24 = 0.05 * jax.random.normal(jax.random.fold_in(_tk, 500 + 24), (1250, 128), jnp.float32)
        tbl_25 = 0.05 * jax.random.normal(jax.random.fold_in(_tk, 500 + 25), (1000, 128), jnp.float32)
        _rk = jax.random.fold_in(_tk, 7)
        r_dense_features = -0.000520686 + 1.00062 * jax.random.normal(jax.random.fold_in(_rk, 101), (512, 128), jnp.float32)
        W_top1 = 0.0405887 * jax.random.normal(jax.random.fold_in(_tk, 801), (607, 512), jnp.float32)
        W_top2 = 0.0441942 * jax.random.normal(jax.random.fold_in(_tk, 802), (512, 256), jnp.float32)
        W_top3 = 0.0625 * jax.random.normal(jax.random.fold_in(_tk, 803), (256, 1), jnp.float32)
        b_top1 = jnp.zeros((512,), jnp.float32)
        b_top2 = jnp.zeros((256,), jnp.float32)
        return (r_dense_features, ids, tbl_0, tbl_1, tbl_2, tbl_3, tbl_4, tbl_5, tbl_6, tbl_7, tbl_8, tbl_9, tbl_10, tbl_11, tbl_12, tbl_13, tbl_14, tbl_15, tbl_16, tbl_17, tbl_18, tbl_19, tbl_20, tbl_21, tbl_22, tbl_23, tbl_24, tbl_25, W_top1, b_top1, W_top2, b_top2, W_top3)
    r_dense_features, ids, tbl_0, tbl_1, tbl_2, tbl_3, tbl_4, tbl_5, tbl_6, tbl_7, tbl_8, tbl_9, tbl_10, tbl_11, tbl_12, tbl_13, tbl_14, tbl_15, tbl_16, tbl_17, tbl_18, tbl_19, tbl_20, tbl_21, tbl_22, tbl_23, tbl_24, tbl_25, W_top1, b_top1, W_top2, b_top2, W_top3 = _rec_inputs()

    def _L0_rec_setup():
        import jax, jax.numpy as jnp
        import numpy as np
        B, F, D = (2048, 26, 128)
        key = jax.random.key(seed)
        k1, k2 = jax.random.split(key)
        dense_features = jax.random.normal(k1, (B, D), dtype=jnp.float32)
        sparse_values = jax.random.normal(k2, (B, F, D), dtype=jnp.float32)
        return {'dense_features': dense_features, 'sparse_values': sparse_values}
    _L0_rec_all = _L0_rec_setup()
    _L0_rec_in = {k: v for k, v in _L0_rec_all.items() if k in ()}
    del _L0_rec_all
    return {'r_dense_features': r_dense_features, 'ids': ids, 'tbl_0': tbl_0, 'tbl_1': tbl_1, 'tbl_2': tbl_2, 'tbl_3': tbl_3, 'tbl_4': tbl_4, 'tbl_5': tbl_5, 'tbl_6': tbl_6, 'tbl_7': tbl_7, 'tbl_8': tbl_8, 'tbl_9': tbl_9, 'tbl_10': tbl_10, 'tbl_11': tbl_11, 'tbl_12': tbl_12, 'tbl_13': tbl_13, 'tbl_14': tbl_14, 'tbl_15': tbl_15, 'tbl_16': tbl_16, 'tbl_17': tbl_17, 'tbl_18': tbl_18, 'tbl_19': tbl_19, 'tbl_20': tbl_20, 'tbl_21': tbl_21, 'tbl_22': tbl_22, 'tbl_23': tbl_23, 'tbl_24': tbl_24, 'tbl_25': tbl_25, 'W_top1': W_top1, 'b_top1': b_top1, 'W_top2': W_top2, 'b_top2': b_top2, 'W_top3': W_top3}

def reference(r_dense_features, ids, tbl_0, tbl_1, tbl_2, tbl_3, tbl_4, tbl_5, tbl_6, tbl_7, tbl_8, tbl_9, tbl_10, tbl_11, tbl_12, tbl_13, tbl_14, tbl_15, tbl_16, tbl_17, tbl_18, tbl_19, tbl_20, tbl_21, tbl_22, tbl_23, tbl_24, tbl_25, W_top1, b_top1, W_top2, b_top2, W_top3):
    import jax
    import jax.numpy as jnp

    def _L0_rec_ref(dense_features, sparse_values):
        import jax, jax.numpy as jnp
        import numpy as np
        B, F, D = (2048, 26, 128)
        sd = jnp.einsum('bfd,bd->bf', sparse_values, dense_features)
        ss = jnp.einsum('bfd,bgd->bfg', sparse_values, sparse_values)
        iu, ju = jnp.triu_indices(F, k=1)
        pairs = ss[:, iu, ju]
        return jnp.concatenate([dense_features, sd, pairs], axis=1)
    e = jnp.stack([tbl_0[ids[:, 0]], tbl_1[ids[:, 1]], tbl_2[ids[:, 2]], tbl_3[ids[:, 3]], tbl_4[ids[:, 4]], tbl_5[ids[:, 5]], tbl_6[ids[:, 6]], tbl_7[ids[:, 7]], tbl_8[ids[:, 8]], tbl_9[ids[:, 9]], tbl_10[ids[:, 10]], tbl_11[ids[:, 11]], tbl_12[ids[:, 12]], tbl_13[ids[:, 13]], tbl_14[ids[:, 14]], tbl_15[ids[:, 15]], tbl_16[ids[:, 16]], tbl_17[ids[:, 17]], tbl_18[ids[:, 18]], tbl_19[ids[:, 19]], tbl_20[ids[:, 20]], tbl_21[ids[:, 21]], tbl_22[ids[:, 22]], tbl_23[ids[:, 23]], tbl_24[ids[:, 24]], tbl_25[ids[:, 25]]], axis=1)
    z = _L0_rec_ref(r_dense_features, e)
    z = z.reshape(z.shape[0], -1)
    h = jnp.concatenate([z, r_dense_features], axis=1)
    h = jnp.maximum(h @ W_top1 + b_top1, 0.0)
    h = jnp.maximum(h @ W_top2 + b_top2, 0.0)
    y = h @ W_top3
    return y

_drawn_inputs = setup_inputs


def setup_inputs(seed=0):
    import zlib

    import numpy as np

    out = dict(_drawn_inputs(seed))
    spreads = {'b_top1': (0.0, 0.1), 'b_top2': (0.0, 0.1)}
    factors = {}
    for name, (base, spread) in spreads.items():
        noise = np.random.default_rng([zlib.crc32(name.encode()), seed]).standard_normal(out[name].shape)
        drawn = base * np.exp(spread * noise) if base else spread * noise
        out[name] = jnp.asarray(drawn.astype(out[name].dtype))
    for name, factor in factors.items():
        out[name] = (out[name] * factor).astype(out[name].dtype)
    return out
```

```python
from contextlib import ExitStack

import concourse.bass as bass
from concourse import mybir

F32 = mybir.dt.float32
I32 = mybir.dt.int32
ALU = mybir.AluOpType
ACT = mybir.ActivationFunctionType

P = 128
QUAD = 4
ROWS = P // QUAD


def interaction_tower(nc, x_T, ids, tables, w_pairs, w_dense, b1, w2, b2, w3, out):
    D, B = x_T.shape
    _, TILES, F = ids.shape
    H1, H2 = w2.shape[1] * P, w2.shape[2]
    KT = w_pairs.shape[1]
    M1, M2 = H1 // P, H2 // P
    GROUPS = [list(range(a, min(a + 4, F))) for a in range(0, F, 4)]
    NG = len(GROUPS)
    QS = P // QUAD
    UNITS = 2
    QU = QS // UNITS
    GBANKS = 3
    NMAX = 256
    MLP = {1: (0, 2 * P), 2: (2 * P, P), 3: (3 * P, P)}
    mlp_nr = {t: n for n, t in enumerate(sorted(MLP))}

    with ExitStack() as ctx:
        def sb(name, shape, dt=F32):
            return ctx.enter_context(nc.sbuf_tensor(name, shape, dt))

        def psum(name, shape):
            return ctx.enter_context(nc.psum_tensor(name, shape, F32))

        def sem(name):
            return ctx.enter_context(nc.semaphore(name))

        ids_sb = sb("ids_sb", [P, TILES, F], I32)
        rows = sb("rows", [P, TILES, F, D])
        feat = sb("feat", [P, B, F + 1])
        prod = sb("prod", [P, KT, B])
        xT = sb("xT", [P, B])
        ident = sb("ident", [P, P])
        wp = sb("wp", [P, KT, H1])
        wd2 = sb("wd2", [P, 2, H1])
        wd = sb("wd", [P, H1])
        w2s = sb("w2s", [P, M1, H2])
        w3s = sb("w3s", [P, M2])
        b1s = sb("b1s", [P, M1])
        b2s = sb("b2s", [P, M2])
        h1 = sb("h1", [P, M1, NMAX])
        h2 = sb("h2", [P, M2, NMAX])
        y = sb("y", [1, B])

        turned = psum("turned", [P, 2, 512])
        gram = psum("gram", [P, GBANKS, 512])
        h1p = psum("h1p", [P, 2, 512])
        h2p = psum("h2p", [P, 512])

        ids_in = sem("ids_in")
        x_in = sem("x_in")
        wd_in = sem("wd_in")
        wp_in = sem("wp_in")
        w2_in = sem("w2_in")
        small_in = sem("small_in")
        gathered = [[sem(f"gathered_{t}_{k}") for k in range(NG)] for t in range(TILES)]
        ident_zero = sem("ident_zero")
        ident_ready = sem("ident_ready")
        pads_zero = sem("pads_zero")
        wd_ready = sem("wd_ready")
        dense_feat = sem("dense_feat")
        turn_done = sem("turn_done")
        feat_ready = sem("feat_ready")
        gram_done = sem("gram_done")
        prod_ready = sem("prod_ready")
        h1_done = sem("h1_done")
        h1_ready = sem("h1_ready")
        h2_done = sem("h2_done")
        h2_ready = sem("h2_ready")
        y_done = sem("y_done")
        y_ready = sem("y_ready")
        y_out = sem("y_out")

        block = ctx.enter_context(nc.Block())

        @block.sync
        def _(sp):
            sp.dma_start(ids_sb[:], ids).then_inc(ids_in, 16)
            sp.dma_start(xT[:], x_T).then_inc(x_in, 16)
            sp.dma_start(wd2[:], w_dense).then_inc(wd_in, 16)
            sp.dma_start(wp[:], w_pairs).then_inc(wp_in, 16)
            sp.dma_start(w2s[:], w2).then_inc(w2_in, 16)
            sp.dma_start(b1s[:], b1).then_inc(small_in, 16)
            sp.dma_start(b2s[:], b2).then_inc(small_in, 16)
            sp.dma_start(w3s[:], w3).then_inc(small_in, 16)
            sp.wait_ge(y_ready, len(MLP))
            sp.dma_start(out, y[:]).then_inc(y_out, 16)
            sp.wait_ge(y_out, 16)

        @block.gpsimd
        def _(pool):
            nc.gpsimd.memset(ident[:], 0.0).then_inc(ident_zero, 1)
            pool.wait_ge(ident_zero, 1)
            nc.gpsimd.affine_select(out=ident[:], in_=ident[:], compare_op=ALU.not_equal, fill=1.0, base=0,
                                    pattern=[[-1, P]], channel_multiplier=1).then_inc(ident_ready, 1)
            pool.wait_ge(ids_in, 16)
            for t in range(TILES):
                for k, group in enumerate(GROUPS):
                    for f in group:
                        pool.indirect_dma_start(
                            out=rows[:, t, f, :], out_offset=None, in_=tables[f],
                            in_offset=bass.IndirectOffsetOnAxis(ap=ids_sb[:, t, f:f + 1], axis=0),
                        ).then_inc(gathered[t][k], 16)

        @block.tensor
        def _(pe):
            def turn(t, k):
                n = t * NG + k
                pe.wait_ge(gathered[t][k], 16 * len(GROUPS[k]))
                if n >= 2:
                    pe.wait_ge(feat_ready, n - 1)
                for i, f in enumerate(GROUPS[k]):
                    last = nc.tensor.transpose(turned[:, n % 2, i * P:(i + 1) * P], rows[:, t, f, :], ident[:])
                last.then_inc(turn_done, 1)

            def products(t, u):
                n = t * UNITS + u
                pe.wait_ge(feat_ready, (t + 1) * NG)
                if n >= GBANKS:
                    pe.wait_ge(prod_ready, n - GBANKS + 1)
                for q in range(QU):
                    for j in range(QUAD):
                        s = t * P + j * QS + u * QU + q
                        last = nc.tensor.matmul(gram[j * ROWS:j * ROWS + F, n % GBANKS, q * F:(q + 1) * F],
                                                feat[:, s, 0:F], feat[:, s, 1:F + 1], start=True, stop=True,
                                                tile_position=(0, j * ROWS))
                last.then_inc(gram_done, 1)

            def layer1(t, half):
                n, (s0, N) = mlp_nr[t], MLP[t]
                pe.wait_ge(prod_ready, (t + 1) * UNITS)
                if n:
                    pe.wait_ge(h1_ready, M1 * (n - 1) + 2 * half + 2)
                for m in (2 * half, 2 * half + 1):
                    to = h1p[:, half, (m % 2) * NMAX:(m % 2) * NMAX + N]
                    cols = slice(m * P, (m + 1) * P)
                    nc.tensor.matmul(to, wd[:, cols], xT[:, s0:s0 + N], start=True, stop=False)
                    for k in range(KT):
                        K = ROWS * min(QUAD, F - QUAD * k)
                        last = nc.tensor.matmul(to, wp[0:K, k, cols], prod[0:K, k, s0:s0 + N],
                                                start=False, stop=(k == KT - 1))
                last.then_inc(h1_done, 1)

            def layer2(t):
                n, (s0, N) = mlp_nr[t], MLP[t]
                pe.wait_ge(h1_ready, M1 * (n + 1))
                if n:
                    pe.wait_ge(y_ready, n)
                for m in range(M2):
                    for k in range(M1):
                        last = nc.tensor.matmul(h2p[:, m * NMAX:m * NMAX + N], w2s[:, k, m * P:(m + 1) * P],
                                                h1[:, k, 0:N], start=(k == 0), stop=(k == M1 - 1))
                last.then_inc(h2_done, 1)

            def layer3(t):
                n, (s0, N) = mlp_nr[t], MLP[t]
                pe.wait_ge(h2_ready, n + 1)
                for k in range(M2):
                    last = nc.tensor.matmul(h2p[0:1, 0:N], w3s[:, k:k + 1], h2[:, k, 0:N],
                                            start=(k == 0), stop=(k == M2 - 1))
                last.then_inc(y_done, 1)

            def behind(t, k):
                if k < UNITS:
                    products(t, k)
                elif t in MLP:
                    if k == 2:
                        if mlp_nr[t] == 0:
                            pe.wait_ge(wd_ready, 1)
                            pe.wait_ge(wp_in, 16)
                        layer1(t, 0)
                    elif k == 3:
                        layer1(t, 1)
                    elif k == 4:
                        if mlp_nr[t] == 0:
                            pe.wait_ge(w2_in, 16)
                        layer2(t)
                    elif k == 5:
                        layer3(t)

            pe.wait_ge(ident_ready, 1)
            for t in range(TILES):
                for k in range(NG):
                    turn(t, k)
                    if t == 0 and k == 0:
                        pe.wait_ge(dense_feat, 1)
                    if t:
                        behind(t - 1, k)
            for k in range(NG):
                behind(TILES - 1, k)

        @block.scalar
        def _(act):
            def copy_turned(t, k):
                n, g = t * NG + k, len(GROUPS[k])
                f0 = GROUPS[k][0] + 1
                act.wait_ge(turn_done, n + 1)
                nc.scalar.copy(feat[:, t * P:(t + 1) * P, f0:f0 + g].rearrange("p s f -> p f s"),
                               turned[:, n % 2, 0:g * P].rearrange("p (f s) -> p f s", s=P)).then_inc(feat_ready, 1)

            def relu1(t, half):
                n, (s0, N) = mlp_nr[t], MLP[t]
                act.wait_ge(h1_done, 2 * n + half + 1)
                if n:
                    act.wait_ge(h2_done, n)
                for m in (2 * half, 2 * half + 1):
                    nc.scalar.activation(h1[:, m, 0:N], h1p[:, half, (m % 2) * NMAX:(m % 2) * NMAX + N],
                                         ACT.Relu, bias=b1s[:, m:m + 1]).then_inc(h1_ready, 1)

            def relu2(t):
                n, (s0, N) = mlp_nr[t], MLP[t]
                act.wait_ge(h2_done, n + 1)
                if n:
                    act.wait_ge(y_done, n)
                for m in range(M2):
                    last = nc.scalar.activation(h2[:, m, 0:N], h2p[:, m * NMAX:m * NMAX + N],
                                                ACT.Relu, bias=b2s[:, m:m + 1])
                last.then_inc(h2_ready, 1)

            def copy_y(t):
                n, (s0, N) = mlp_nr[t], MLP[t]
                act.wait_ge(y_done, n + 1)
                nc.scalar.copy(y[:, s0:s0 + N], h2p[0:1, 0:N]).then_inc(y_ready, 1)

            def behind(t, k):
                if t in MLP:
                    if k == 2:
                        relu1(t, 0)
                    elif k == 3:
                        relu1(t, 1)
                    elif k == 4:
                        relu2(t)
                    elif k == 5:
                        copy_y(t)

            act.wait_ge(x_in, 16)
            nc.scalar.copy(feat[:, :, 0], xT[:]).then_inc(dense_feat, 1)
            act.wait_ge(small_in, 48)
            for t in range(TILES):
                for k in range(NG):
                    copy_turned(t, k)
                    if t:
                        behind(t - 1, k)
            for k in range(NG):
                behind(TILES - 1, k)

        @block.vector
        def _(dve):
            nc.vector.memset(prod[:], 0.0).then_inc(pads_zero, 1)
            dve.wait_ge(wd_in, 16)
            nc.vector.tensor_tensor(wd[:], wd2[:, 0, :], wd2[:, 1, :], ALU.add).then_inc(wd_ready, 1)
            dve.wait_ge(pads_zero, 1)
            for t in range(TILES):
                for u in range(UNITS):
                    n = t * UNITS + u
                    dve.wait_ge(gram_done, n + 1)
                    unit = gram[:, n % GBANKS, 0:QU * F].rearrange("p (q g) -> p g q", g=F)
                    for j in range(QUAD):
                        s0 = t * P + j * QS + u * QU
                        for i in range(QUAD):
                            g = len(range(i, F, QUAD))
                            last = nc.vector.tensor_copy(prod[i * ROWS:i * ROWS + F, 0:g, s0:s0 + QU],
                                                         unit[j * ROWS:j * ROWS + F, i:F:QUAD, :])
                    last.then_inc(prod_ready, 1)


_TABLES = [f"tbl_{f}" for f in range(26)]


def kernel(**inputs):
    import numpy as _np
    import concourse.bacc as _bacc
    from concourse import mybir as _mybir
    from concourse.bass_utils import run_bass_kernel_spmd as _run

    x, ids, W1 = inputs["r_dense_features"], inputs["ids"], inputs["W_top1"]
    W2, W3 = inputs["W_top2"], inputs["W_top3"]
    B, D = x.shape
    F = ids.shape[1]
    H1, H2 = W2.shape
    kt = -(-F // 4)
    slot = _np.zeros((P, kt), _np.int64)
    used = _np.zeros((P, kt), bool)
    row = D
    for f in range(F):
        for g in range(f + 1, F + 1):
            at = 32 * ((g - 1) % 4) + f, (g - 1) // 4
            slot[at], used[at] = row, True
            row += 1
    wp = _np.zeros((P, kt, H1), W1.dtype)
    wp[used] = _np.asarray(W1)[slot[used]]
    laid_out = {
        "x_T": _np.asarray(x).T,
        "ids": _np.asarray(ids).reshape(B // P, P, F).transpose(1, 0, 2),
        **{n: inputs[n] for n in _TABLES},
        "w_pairs": wp,
        "w_dense": _np.stack([W1[:D], W1[row:]], axis=1),
        "b1": _np.asarray(inputs["b_top1"]).reshape(H1 // P, P).T,
        "w2": _np.asarray(W2).reshape(H1 // P, P, H2).transpose(1, 0, 2),
        "b2": _np.asarray(inputs["b_top2"]).reshape(H2 // P, P).T,
        "w3": _np.asarray(W3).reshape(H2 // P, P).T,
    }
    nc = _bacc.Bacc("TRN2", target_bir_lowering=False, num_devices=1)
    arrays, aps = {}, {}
    for name, a in laid_out.items():
        a = _np.ascontiguousarray(a)
        arrays[f"in_{name}"] = a
        aps[name] = nc.dram_tensor(f"in_{name}", a.shape, _mybir.dt.from_np(a.dtype), kind="ExternalInput").ap()
    out = nc.dram_tensor("out", (1, B), F32, kind="ExternalOutput").ap()
    interaction_tower(nc, aps["x_T"], aps["ids"], [aps[n] for n in _TABLES], aps["w_pairs"], aps["w_dense"],
                      aps["b1"], aps["w2"], aps["b2"], aps["w3"], out)
    r = _run(nc, [arrays], core_ids=[0])
    return r.results[0]["out"].reshape(B, 1)
```

```python
from contextlib import ExitStack

import concourse.bass as bass
from concourse import mybir

F32 = mybir.dt.float32
F32R = mybir.dt.float32r
I32 = mybir.dt.int32
ALU = mybir.AluOpType
ACT = mybir.ActivationFunctionType

P = 128
QUAD = 4
ROWS = P // QUAD


def slots_of(places):
    half = places // 2
    return half + 1, [range(c + 1, c + 1 + half) for c in range(half)]


def interaction_tower(nc, x_T, ids, ids_looked, looked, gathered, first_column, w_pairs, w_dense, b1, w2, b2, w3,
                      out):
    D, B = x_T.shape
    _, TILES, NGATH = ids.shape
    NLOOK = len(looked)
    C = NLOOK + NGATH + 1
    SLOTS, _ = slots_of(C)
    H1, H2 = w2.shape[1] * P, w2.shape[2]
    KT = w_pairs.shape[1]
    M1, M2 = H1 // P, H2 // P
    LAST = TILES - 1
    GROUPS = [list(range(a, min(a + QUAD, C))) for a in range(NLOOK + 1, C, QUAD)]
    NG = len(GROUPS)
    QS = P // QUAD
    UNITS = 2
    QU = QS // UNITS
    GBANKS = 3
    DVE_SHARE, ACT_SHARE = (0, 1, 2), (3,)
    CH = [-(-table.shape[0] // P) for table in looked]
    LP = [table.shape[0] // c for table, c in zip(looked, CH)]
    assert all(c * p == table.shape[0] for table, c, p in zip(looked, CH, LP))

    AFTER = {
        (0, 0): [("look", 1)], (0, 2): [("look", 2)], (0, 3): [("look", 3)],
        (1, 0): [("look", 4)], (1, 2): [("look", 5), ("products", 0)],
        (1, 4): [("products", 1)],
        (2, 0): [("layer1", 0)], (2, 1): [("layer2", 0), ("layer3", 0), ("layer1", 1)],
        (2, 2): [("layer2", 1), ("layer3", 1)],
        (2, 4): [("products", 2)],
        (3, 1): [("layer1", 2)], (3, 2): [("layer2", 2), ("layer3", 2)],
        (3, 4): [("products", 3), ("layer1", 3), ("layer2", 3), ("layer3", 3)],
    }
    turns = [("turn", t, k) for t in range(TILES) for k in range(NG)]
    order = [("look", 0)] + [step for turn in turns for step in [turn, *AFTER.get(turn[1:], [])]]
    passes = [step for step in order if step[0] in ("turn", "look")]
    pass_nr = {step: n for n, step in enumerate(passes)}
    assert sum(step[0] == "look" for step in passes) == NLOOK

    with ExitStack() as ctx:
        def sb(name, shape, dt=F32):
            return ctx.enter_context(nc.sbuf_tensor(name, shape, dt))

        def psum(name, shape):
            return ctx.enter_context(nc.psum_tensor(name, shape, F32))

        def sem(name):
            return ctx.enter_context(nc.semaphore(name))

        ids_sb = sb("ids_sb", [P, TILES, NGATH], I32)
        rows = sb("rows", [P, TILES, NGATH, D])
        feat = sb("feat", [P, B, C])
        picked = sb("picked", [P, 2, SLOTS, QS])
        prod = sb("prod", [P, KT, B])
        first = sb("first", [P, SLOTS - 1], I32)
        xT = sb("xT", [P, B])
        ident = sb("ident", [P, P])
        idl = sb("idl", [P, NLOOK, B], I32)
        rownr = {c: sb(f"rownr_{c}", [P, c], I32) for c in sorted(set(CH))}
        onehot = sb("onehot", [P, 2, max(CH), B], F32R)
        tab = sb("tab", [P, 2, max(CH), D])
        high = sb("high", [P, 2, max(CH), D], F32R)
        low = sb("low", [P, 2, max(CH), D], F32R)
        wp = sb("wp", [P, KT, H1])
        wd2 = sb("wd2", [P, 2, H1])
        wd = wd2[:, 0, :]
        w2s = sb("w2s", [P, M1, H2])
        w3s = sb("w3s", [P, M2])
        b1s = sb("b1s", [P, M1])
        b2s = sb("b2s", [P, M2])
        h1 = sb("h1", [P, M1, P])
        h2 = sb("h2", [P, M2, P])
        y = sb("y", [1, B])

        turned = psum("turned", [P, 2, 512])
        gram = psum("gram", [P, GBANKS, 512])
        h1p = psum("h1p", [P, 2, 512])
        h2p = psum("h2p", [P, 512])

        ids_in = sem("ids_in")
        idl_in = [sem(f"idl_in_{e}") for e in range(NLOOK)]
        tab_in = [sem(f"tab_in_{e}") for e in range(NLOOK)]
        x_in = sem("x_in")
        wd_in = sem("wd_in")
        wp_in = sem("wp_in")
        w2_in = sem("w2_in")
        small_in = sem("small_in")
        first_in = sem("first_in")
        rows_in = [[sem(f"rows_in_{t}_{k}") for k in range(NG)] for t in range(TILES)]
        ident_zero = sem("ident_zero")
        ident_ready = sem("ident_ready")
        rownr_ready = sem("rownr_ready")
        gram_zero = sem("gram_zero")
        wd_ready = sem("wd_ready")
        dense_feat = sem("dense_feat")
        onehot_ready = sem("onehot_ready")
        high_ready = sem("high_ready")
        low_ready = sem("low_ready")
        turn_done = sem("turn_done")
        feat_ready = sem("feat_ready")
        gram_done = sem("gram_done")
        second_picked = sem("second_picked")
        unit_picked = sem("unit_picked")
        prod_ready = sem("prod_ready")
        prod_ready_dve = sem("prod_ready_dve")
        h1_done = sem("h1_done")
        h1_ready = sem("h1_ready")
        h2_done = sem("h2_done")
        h2_ready = sem("h2_ready")
        y_done = sem("y_done")
        y_ready = sem("y_ready")
        y_out = sem("y_out")

        block = ctx.enter_context(nc.Block())

        @block.sync
        def _(sp):
            def load_table(e):
                sp.dma_start(idl[0:LP[e], e], ids_looked[e:e + 1].to_broadcast([LP[e], B])).then_inc(idl_in[e], 16)
                if e >= 2:
                    sp.wait_ge(low_ready, e - 1)
                sp.dma_start(tab[0:LP[e], e % 2, 0:CH[e]],
                             looked[e].rearrange("(p c) d -> p c d", c=CH[e])).then_inc(tab_in[e], 16)

            sp.dma_start(ids_sb[:], ids).then_inc(ids_in, 16)
            load_table(0)
            sp.dma_start(xT[:], x_T).then_inc(x_in, 16)
            load_table(1)
            sp.dma_start(wd2[:], w_dense).then_inc(wd_in, 16)
            sp.dma_start(first[:], first_column).then_inc(first_in, 16)
            load_table(2)
            load_table(3)
            sp.dma_start(b1s[:], b1).then_inc(small_in, 16)
            sp.dma_start(b2s[:], b2).then_inc(small_in, 16)
            sp.dma_start(w3s[:], w3).then_inc(small_in, 16)
            sp.dma_start(wp[:], w_pairs).then_inc(wp_in, 16)
            sp.dma_start(w2s[:], w2).then_inc(w2_in, 16)
            for e in range(4, NLOOK):
                load_table(e)
            sp.wait_ge(y_ready, TILES)
            sp.dma_start(out, y[:]).then_inc(y_out, 16)
            sp.wait_ge(y_out, 16)

        @block.gpsimd
        def _(pool):
            nc.gpsimd.memset(ident[:], 0.0).then_inc(ident_zero, 1)
            for c, numbers in rownr.items():
                nc.gpsimd.iota(numbers[:], pattern=[[1, c]], base=0, channel_multiplier=c).then_inc(rownr_ready, 1)
            pool.wait_ge(ident_zero, 1)
            nc.gpsimd.affine_select(out=ident[:], in_=ident[:], compare_op=ALU.not_equal, fill=1.0, base=0,
                                    pattern=[[-1, P]], channel_multiplier=1).then_inc(ident_ready, 1)
            pool.wait_ge(ids_in, 16)
            for t in range(TILES):
                for k, group in enumerate(GROUPS):
                    for f in group:
                        g = f - NLOOK - 1
                        pool.indirect_dma_start(
                            out=rows[:, t, g, :], out_offset=None, in_=gathered[g],
                            in_offset=bass.IndirectOffsetOnAxis(ap=ids_sb[:, t, g:g + 1], axis=0),
                        ).then_inc(rows_in[t][k], 16)

        @block.tensor
        def _(pe):
            def bank_free(n):
                if n >= 2:
                    pe.wait_ge(feat_ready, n - 1)

            def turn(t, k):
                n = pass_nr["turn", t, k]
                pe.wait_ge(rows_in[t][k], 16 * len(GROUPS[k]))
                bank_free(n)
                for i, f in enumerate(GROUPS[k]):
                    last = nc.tensor.transpose(turned[:, n % 2, i * P:(i + 1) * P], rows[:, t, f - NLOOK - 1, :],
                                               ident[:])
                last.then_inc(turn_done, 1)

            def look(e):
                n = pass_nr["look", e]
                bank_free(n)
                pe.wait_ge(onehot_ready, e + 1)
                for part, ready in ((high, high_ready), (low, low_ready)):
                    pe.wait_ge(ready, e + 1)
                    for c in range(CH[e]):
                        last = nc.tensor.matmul(turned[:, n % 2, :], part[0:LP[e], e % 2, c, :],
                                                onehot[0:LP[e], e % 2, c, :], start=(part is high and c == 0),
                                                stop=(part is low and c == CH[e] - 1))
                last.then_inc(turn_done, 1)

            def products(t):
                pe.wait_ge(feat_ready, max(nr for step, nr in pass_nr.items() if step[0] == "look" or step[1] == t) + 1)
                for u in range(UNITS):
                    n = t * UNITS + u
                    if n >= GBANKS:
                        pe.wait_ge(unit_picked, n - GBANKS + 1)
                    for q in range(QU):
                        for j in range(QUAD):
                            sample = feat[:, t * P + j * QS + u * QU + q, :]
                            last = nc.tensor.matmul(gram[j * ROWS:j * ROWS + C, n % GBANKS, q * C:(q + 1) * C],
                                                    sample, sample, start=True, stop=True,
                                                    tile_position=(0, j * ROWS))
                    last.then_inc(gram_done, 1)

            def layer1(t):
                samples = slice(t * P, (t + 1) * P)
                for half in range(2):
                    if t:
                        pe.wait_ge(h1_ready, M1 * (t - 1) + 2 * half + 2)
                    for m in (0, 1):
                        cols = slice((2 * half + m) * P, (2 * half + m + 1) * P)
                        nc.tensor.matmul(h1p[:, half, m * P:(m + 1) * P], wd[:, cols], xT[:, samples],
                                         start=(m == 0), stop=False, skip_group_check=True)
                pe.wait_ge(prod_ready, t + 1)
                pe.wait_ge(prod_ready_dve, t + 1)
                for half in range(2):
                    for m in (0, 1):
                        cols = slice((2 * half + m) * P, (2 * half + m + 1) * P)
                        for k in range(KT):
                            K = ROWS * min(QUAD, SLOTS - QUAD * k)
                            last = nc.tensor.matmul(h1p[:, half, m * P:(m + 1) * P], wp[0:K, k, cols],
                                                    prod[0:K, k, samples], start=False, stop=(k == KT - 1),
                                                    skip_group_check=True)
                    last.then_inc(h1_done, 1)

            def layer2(t):
                if t:
                    pe.wait_ge(y_ready, t)
                for m in range(M2):
                    for k in range(M1):
                        if m == 0:
                            pe.wait_ge(h1_ready, M1 * t + k + 1)
                        last = nc.tensor.matmul(h2p[:, m * P:(m + 1) * P], w2s[:, k, m * P:(m + 1) * P],
                                                h1[:, k, :], start=(k == 0), stop=(k == M1 - 1))
                last.then_inc(h2_done, 1)

            def layer3(t):
                pe.wait_ge(h2_ready, t + 1)
                for k in range(M2):
                    last = nc.tensor.matmul(h2p[0:1, 0:P], w3s[:, k:k + 1], h2[:, k, :],
                                            start=(k == 0), stop=(k == M2 - 1))
                last.then_inc(y_done, 1)

            pe.wait_ge(ident_ready, 1)
            for what, *at in order:
                if what == "turn":
                    turn(*at)
                elif what == "look":
                    look(*at)
                elif what == "products":
                    if at == [0]:
                        pe.wait_ge(dense_feat, 1)
                        pe.wait_ge(gram_zero, 1)
                    products(*at)
                elif what == "layer1":
                    if at == [0]:
                        pe.wait_ge(wd_ready, 1)
                        pe.wait_ge(wp_in, 16)
                    layer1(*at)
                elif what == "layer2":
                    if at == [0]:
                        pe.wait_ge(w2_in, 16)
                        pe.wait_ge(small_in, 48)
                    layer2(*at)
                elif what == "layer3":
                    layer3(*at)

        def spread(copy, t, quadrants, units):
            q0, q1 = units.start * QU, units.stop * QU
            for j in quadrants:
                s0 = t * P + j * QS
                for i in range(QUAD):
                    k = len(range(i, SLOTS, QUAD))
                    last = copy(prod[i * ROWS:(i + 1) * ROWS, 0:k, s0 + q0:s0 + q1],
                                picked[j * ROWS:(j + 1) * ROWS, t % 2, i:SLOTS:QUAD, q0:q1])
            return last

        def together(t):
            return [range(UNITS)] if t < LAST else [range(u, u + 1) for u in range(UNITS)]

        @block.scalar
        def _(act):
            def round_table(e):
                act.wait_ge(tab_in[e], 16)
                if e >= 2:
                    act.wait_ge(turn_done, pass_nr["look", e - 2] + 1)
                nc.scalar.copy(high[0:LP[e], e % 2, 0:CH[e], :], tab[0:LP[e], e % 2, 0:CH[e], :]
                               ).then_inc(high_ready, 1)

            def copy_turned(t, k):
                n, g, f0 = pass_nr["turn", t, k], len(GROUPS[k]), GROUPS[k][0]
                act.wait_ge(turn_done, n + 1)
                nc.scalar.copy(feat[:, t * P:(t + 1) * P, f0:f0 + g].rearrange("p s f -> p f s"),
                               turned[:, n % 2, 0:g * P].rearrange("p (f s) -> p f s", s=P)).then_inc(feat_ready, 1)

            def copy_looked(e):
                n = pass_nr["look", e]
                act.wait_ge(turn_done, n + 1)
                nc.scalar.copy(feat[:, :, e + 1], turned[:, n % 2, 0:B]).then_inc(feat_ready, 1)

            def spread_tile(t):
                for units in together(t):
                    act.wait_ge(unit_picked, t * UNITS + units.stop)
                    last = spread(nc.scalar.copy, t, ACT_SHARE, units)
                last.then_inc(prod_ready, 1)

            def relu1(t):
                if t:
                    act.wait_ge(h2_done, t)
                for m in range(M1):
                    if m % 2 == 0:
                        act.wait_ge(h1_done, 2 * t + m // 2 + 1)
                    nc.scalar.activation(h1[:, m, :], h1p[:, m // 2, (m % 2) * P:(m % 2 + 1) * P],
                                         ACT.Relu, bias=b1s[:, m:m + 1]).then_inc(h1_ready, 1)

            def relu2(t):
                act.wait_ge(h2_done, t + 1)
                if t:
                    act.wait_ge(y_done, t)
                for m in range(M2):
                    last = nc.scalar.activation(h2[:, m, :], h2p[:, m * P:(m + 1) * P],
                                                ACT.Relu, bias=b2s[:, m:m + 1])
                last.then_inc(h2_ready, 1)

            def copy_y(t):
                act.wait_ge(y_done, t + 1)
                nc.scalar.copy(y[:, t * P:(t + 1) * P], h2p[0:1, 0:P]).then_inc(y_ready, 1)

            round_table(0)
            act.wait_ge(x_in, 16)
            nc.scalar.copy(feat[:, :, 0], xT[:]).then_inc(dense_feat, 1)
            round_table(1)
            for what, *at in order:
                if what == "turn":
                    copy_turned(*at)
                elif what == "look":
                    copy_looked(*at)
                    if at[0] + 2 < NLOOK:
                        round_table(at[0] + 2)
                elif what == "products":
                    spread_tile(*at)
                elif what == "layer1":
                    if at == [0]:
                        act.wait_ge(small_in, 48)
                    relu1(*at)
                elif what == "layer2":
                    relu2(*at)
                elif what == "layer3":
                    copy_y(*at)

        @block.vector
        def _(dve):
            def build_onehot(e):
                dve.wait_ge(idl_in[e], 16)
                if e >= 2:
                    dve.wait_ge(turn_done, pass_nr["look", e - 2] + 1)
                for c in range(CH[e]):
                    last = nc.vector.tensor_tensor(onehot[0:LP[e], e % 2, c, :], idl[0:LP[e], e, :],
                                                   rownr[CH[e]][0:LP[e], c:c + 1].to_broadcast([LP[e], B]),
                                                   ALU.is_equal)
                last.then_inc(onehot_ready, 1)

            def split_table(e):
                used = (slice(0, LP[e]), e % 2, slice(0, CH[e]))
                dve.wait_ge(high_ready, e + 1)
                nc.vector.tensor_tensor(low[used], tab[used], high[used].bitcast(F32), ALU.subtract
                                        ).then_inc(low_ready, 1)

            def pick(t, u):
                n = t * UNITS + u
                if t >= 2 and u == 0:
                    dve.wait_ge(prod_ready, t - 1)
                    dve.wait_ge(prod_ready_dve, t - 1)
                dve.wait_ge(gram_done, n + 1)
                unit = gram[:, n % GBANKS, 0:QU * C].rearrange("p (q c) -> p c q", c=C)
                to = picked[:, t % 2, :, u * QU:(u + 1) * QU]
                nc.vector.tensor_copy(to, unit[:, SLOTS - 1:C, :]).then_inc(second_picked, 1)
                dve.wait_ge(second_picked, n + 1)
                mask = first[:].rearrange("p (c o) -> p c o", o=1).to_broadcast([P, SLOTS - 1, QU])
                nc.vector.copy_predicated(to[:, 0:SLOTS - 1, :], mask, unit[:, 0:SLOTS - 1, :]
                                          ).then_inc(unit_picked, 1)

            nc.vector.memset(gram[:], 0.0).then_inc(gram_zero, 1)
            dve.wait_ge(rownr_ready, len(rownr))
            for e in range(NLOOK):
                build_onehot(e)
                split_table(e)
            dve.wait_ge(wd_in, 16)
            nc.vector.tensor_tensor(wd, wd, wd2[:, 1, :], ALU.add).then_inc(wd_ready, 1)
            dve.wait_ge(first_in, 16)
            dve.wait_ge(gram_zero, 1)
            for t in range(TILES):
                for units in together(t):
                    for u in units:
                        pick(t, u)
                    dve.wait_ge(unit_picked, t * UNITS + units.stop)
                    last = spread(nc.vector.tensor_copy, t, DVE_SHARE, units)
                last.then_inc(prod_ready_dve, 1)


_LOOKED = [3, 6, 13, 17, 19, 25]
_PLACES = _LOOKED + [f for f in range(26) if f not in _LOOKED]


def kernel(**inputs):
    import numpy as _np
    import concourse.bacc as _bacc
    from concourse import mybir as _mybir
    from concourse.bass_utils import run_bass_kernel_spmd as _run

    x, ids, W1 = (_np.asarray(inputs[n]) for n in ("r_dense_features", "ids", "W_top1"))
    W2, W3 = inputs["W_top2"], inputs["W_top3"]
    B, D = x.shape
    F = ids.shape[1]
    NL = len(_LOOKED)
    H1, H2 = W2.shape
    place = [0] + [_PLACES.index(f) + 1 for f in range(F)]
    slots, first_rows = slots_of(F + 1)
    at, row = [], D
    for a in range(F):
        for b in range(a + 1, F + 1):
            c, r = place[a], place[b]
            if (r - c) % (F + 1) >= slots:
                c, r = r, c
            slot = c if c < slots - 1 else c - (slots - 1)
            at.append((ROWS * (slot % QUAD) + r, slot // QUAD))
            row += 1
    assert len(set(at)) == len(at)
    w_pairs = _np.zeros((P, -(-slots // QUAD), H1), W1.dtype)
    w_pairs[tuple(_np.array(at).T)] = W1[D:row]
    first = _np.zeros((QUAD, ROWS, slots - 1), _np.int32)
    for c, rows in enumerate(first_rows):
        first[:, list(rows), c] = 1
    laid_out = {
        "x_T": x.T,
        "ids": ids[:, _PLACES[NL:]].reshape(B // P, P, F - NL).transpose(1, 0, 2),
        "ids_looked": ids[:, _LOOKED].T,
        **{f"tbl_{f}": inputs[f"tbl_{f}"] for f in range(F)},
        "first_column": first.reshape(P, slots - 1),
        "w_pairs": w_pairs,
        "w_dense": _np.stack([W1[:D], W1[row:]], axis=1),
        "b1": _np.asarray(inputs["b_top1"]).reshape(H1 // P, P).T,
        "w2": _np.asarray(W2).reshape(H1 // P, P, H2).transpose(1, 0, 2),
        "b2": _np.asarray(inputs["b_top2"]).reshape(H2 // P, P).T,
        "w3": _np.asarray(W3).reshape(H2 // P, P).T,
    }
    nc = _bacc.Bacc("TRN2", target_bir_lowering=False, num_devices=1)
    arrays, aps = {}, {}
    for name, a in laid_out.items():
        a = _np.ascontiguousarray(a)
        arrays[f"in_{name}"] = a
        aps[name] = nc.dram_tensor(f"in_{name}", a.shape, _mybir.dt.from_np(a.dtype), kind="ExternalInput").ap()
    out = nc.dram_tensor("out", (1, B), F32, kind="ExternalOutput").ap()
    tables = [aps[f"tbl_{f}"] for f in _PLACES]
    interaction_tower(nc, aps["x_T"], aps["ids"], aps["ids_looked"], tables[:NL], tables[NL:],
                      aps["first_column"], aps["w_pairs"], aps["w_dense"], aps["b1"], aps["w2"], aps["b2"],
                      aps["w3"], out)
    r = _run(nc, [arrays], core_ids=[0])
    return r.results[0]["out"].reshape(B, 1)
```

```python
from contextlib import ExitStack

import concourse.bass as bass
from concourse import mybir

F32 = mybir.dt.float32
F32R = mybir.dt.float32r
I32 = mybir.dt.int32
ALU = mybir.AluOpType
ACT = mybir.ActivationFunctionType

P = 128
QUAD = 4
ROWS = P // QUAD


def slots_of(places):
    half = places // 2
    return half + 1, [range(c + 1, c + 1 + half) for c in range(half)]


def interaction_tower(nc, x_T, ids, ids_looked, looked, gathered, places, first_column, w_pairs, w_dense,
                      b1, w2, b2, w3, out):
    D, B = x_T.shape
    _, TILES, NGATH = ids.shape
    NLOOK = len(looked)
    C = places
    NFULL = C - 1 - NGATH
    SLOTS, _ = slots_of(C)
    H1, H2 = w2.shape[1] * P, w2.shape[2]
    KT = w_pairs.shape[1]
    M1, M2 = H1 // P, H2 // P
    LAST = TILES - 1
    LATE = TILES // 2
    FROM = [0 if e < NFULL else LATE for e in range(NLOOK)]
    GROUPS = []
    for t in range(TILES):
        starts = {*range(1 + (NFULL if t < LATE else NLOOK), C, QUAD), C}
        if t == LAST:
            starts.add(C - 1)
        starts = sorted(starts)
        GROUPS.append([list(range(a, b)) for a, b in zip(starts, starts[1:])])
    QS = P // QUAD
    UNITS = 2
    QU = QS // UNITS
    GBANKS = 2
    TBANKS = 3
    SPREAD = [(j, i) for j in range(QUAD) for i in range(QUAD)]
    DVE_SHARE = [[12]] * LAST + [[5, 9]]
    CH = [-(-table.shape[0] // P) for table in looked]
    LP = [table.shape[0] // c for table, c in zip(looked, CH)]
    assert all(c * p == table.shape[0] for table, c, p in zip(looked, CH, LP))

    ACT_CHUNKS = 2
    DVE_CHUNKS = 3

    def DENSE(t):
        return [("dense", t, half) for half in range(2)]

    def LAYER1(t):
        return [("layer1", t, half) for half in range(2)]

    START = [("build", 0), ("build", 1), ("copy_dense",), ("look", 0), ("build", 2)]
    AFTER = {
        (0, 0): [("look", 1), ("build", 3)],
        (0, 1): [("look", 2), ("build", 4)],
        (0, 2): [("look", 3), ("build", 5)],
        (0, 3): [("look", 4)],
        (0, 4): [("look", 5), ("sum_dense",), ("build", 6)],
        (1, 1): [*DENSE(0), ("products", 0)],
        (1, 2): [("look", 6), ("build", 7)],
        (1, 3): [*LAYER1(0)],
        (1, 4): [("layer2", 0), ("products", 1), ("build", 8)],
        (2, 0): [*DENSE(1), ("layer3", 0), ("look", 7), ("build", 9), *LAYER1(1)],
        (2, 1): [("look", 8)],
        (2, 2): [("look", 9)],
        (2, 3): [*DENSE(2), ("products", 2)],
        (3, 0): [("layer2", 1)],
        (3, 1): [("layer1", 2, 0), ("layer3", 1)],
        (3, 2): [("layer1", 2, 1)],
        (3, 3): [("dense", 3, 0)],
        (3, 4): [("dense", 3, 1), ("products", 3), ("layer2", 2), ("layer1", 3, 0), ("layer3", 2),
                 ("layer1", 3, 1), ("layer2", 3), ("layer3", 3)],
    }
    turns = [("turn", t, k) for t in range(TILES) for k in range(len(GROUPS[t]))]
    order = START + [step for turn in turns for step in [turn, *AFTER.get(turn[1:], [])]]
    passes = [step for step in order if step[0] in ("turn", "look")]
    pass_nr = {step: n for n, step in enumerate(passes)}
    assert [step for step in passes if step[0] == "look"] == [("look", e) for e in range(NLOOK)]

    with ExitStack() as ctx:
        def sb(name, shape, dt=F32):
            return ctx.enter_context(nc.sbuf_tensor(name, shape, dt))

        def psum(name, shape):
            return ctx.enter_context(nc.psum_tensor(name, shape, F32))

        def sem(name):
            return ctx.enter_context(nc.semaphore(name))

        ids_sb = sb("ids_sb", [P, TILES, NGATH], I32)
        rows = sb("rows", [P, 2, NGATH, D])
        feat = sb("feat", [P, B, C])
        picked = sb("picked", [P, 2, SLOTS, QS])
        prod = sb("prod", [P, KT, B])
        first = sb("first", [P, SLOTS - 1], I32)
        xT = sb("xT", [P, B])
        ident = sb("ident", [P, P])
        idl = sb("idl", [P, 3, B], I32)
        rownr = {c: sb(f"rownr_{c}", [P, c], I32) for c in sorted(set(CH))}
        rownr_f = {c: sb(f"rownr_f_{c}", [P, c]) for c in rownr}
        one = sb("one", [P, 1])
        distance = sb("distance", [P, ACT_CHUNKS, B])
        onehot = sb("onehot", [P, 2, max(CH), B], F32R)
        tab = sb("tab", [P, 2, max(CH), D])
        high = sb("high", [P, 2, max(CH), D], F32R)
        low = sb("low", [P, 2, max(CH), D], F32R)
        wp = sb("wp", [P, KT, H1])
        wd2 = sb("wd2", [P, 2, H1])
        wd = wd2[:, 0, :]
        w2s = sb("w2s", [P, M1, H2])
        w3s = sb("w3s", [P, M2])
        b1s = sb("b1s", [P, M1])
        b2s = sb("b2s", [P, M2])
        h1 = sb("h1", [P, M1, P])
        h2 = sb("h2", [P, M2, P])
        y = sb("y", [1, B])

        turned = psum("turned", [P, TBANKS, 512])
        gram = psum("gram", [P, GBANKS, 512])
        h1p = psum("h1p", [P, 2, 512])
        h2p = psum("h2p", [P, 512])

        ids_in = sem("ids_in")
        idl_in = [sem(f"idl_in_{e}") for e in range(NLOOK)]
        tab_in = [sem(f"tab_in_{e}") for e in range(NLOOK)]
        x_in = sem("x_in")
        wd_in = sem("wd_in")
        wp_in = sem("wp_in")
        w2_in = sem("w2_in")
        small_in = sem("small_in")
        first_in = sem("first_in")
        rows_in = [[sem(f"rows_in_{t}_{k}") for k in range(len(GROUPS[t]))] for t in range(TILES)]
        ident_zero = sem("ident_zero")
        ident_ready = sem("ident_ready")
        rownr_ready = sem("rownr_ready")
        gram_zero = sem("gram_zero")
        wd_ready = sem("wd_ready")
        dense_feat = sem("dense_feat")
        rownr_f_ready = sem("rownr_f_ready")
        one_ready = sem("one_ready")
        onehot_ready = sem("onehot_ready")
        onehot_ready_act = sem("onehot_ready_act")
        distance_ready = sem("distance_ready")
        high_ready = sem("high_ready")
        low_ready = sem("low_ready")
        turn_done = sem("turn_done")
        feat_ready = sem("feat_ready")
        gram_done = sem("gram_done")
        second_picked = sem("second_picked")
        unit_picked = sem("unit_picked")
        prod_ready = sem("prod_ready")
        prod_ready_dve = sem("prod_ready_dve")
        h1_done = sem("h1_done")
        h1_ready = sem("h1_ready")
        h2_done = sem("h2_done")
        h2_ready = sem("h2_ready")
        y_done = sem("y_done")
        y_ready = sem("y_ready")
        y_out = sem("y_out")

        def dve_builds(e):
            return sum(-(-(chunks - ACT_CHUNKS) // DVE_CHUNKS) for chunks in CH[:e])

        def looked_samples(e):
            return slice(FROM[e] * P, B)

        def h1_tile(t, m):
            if t == LAST and m == M1 - 1:
                return turned[:, len(passes) % TBANKS, 0:P]
            return h1p[:, m // 2, (m % 2) * P:(m % 2 + 1) * P]

        def h2_tile(t, m):
            if t == LAST and m == M2 - 1:
                return turned[:, (len(passes) + 1) % TBANKS, 0:P]
            return h2p[:, m * P:(m + 1) * P]

        block = ctx.enter_context(nc.Block())

        @block.sync
        def _(sp):
            def load_table(e):
                if e >= 3:
                    sp.wait_ge(onehot_ready, dve_builds(e - 2))
                    sp.wait_ge(distance_ready, e - 2)
                samples = looked_samples(e)
                sp.dma_start(idl[0:LP[e], e % 3, samples],
                             ids_looked[e:e + 1, samples].to_broadcast([LP[e], B - samples.start])
                             ).then_inc(idl_in[e], 16)
                if e >= 2:
                    sp.wait_ge(low_ready, e - 1)
                sp.dma_start(tab[0:LP[e], e % 2, 0:CH[e]],
                             looked[e].rearrange("(p c) d -> p c d", c=CH[e])).then_inc(tab_in[e], 16)

            sp.dma_start(ids_sb[:], ids).then_inc(ids_in, 16)
            for e in range(NLOOK):
                load_table(e)
                if e == 1:
                    sp.dma_start(xT[:], x_T).then_inc(x_in, 16)
                elif e == 3:
                    sp.dma_start(wd2[:], w_dense).then_inc(wd_in, 16)
                    sp.dma_start(first[:], first_column).then_inc(first_in, 16)
                elif e == 5:
                    for k in range(KT):
                        sp.dma_start(wp[:, k], w_pairs[:, k]).then_inc(wp_in, 16)
                elif e == 7:
                    sp.dma_start(b1s[:], b1).then_inc(small_in, 16)
                    sp.dma_start(b2s[:], b2).then_inc(small_in, 16)
                    sp.dma_start(w3s[:], w3).then_inc(small_in, 16)
                    sp.dma_start(w2s[:], w2).then_inc(w2_in, 16)
            sp.wait_ge(y_ready, TILES)
            sp.dma_start(out, y[:]).then_inc(y_out, 16)
            sp.wait_ge(y_out, 16)

        def spread(copy, t, share, units):
            q0, q1 = units.start * QU, units.stop * QU
            for j, i in share:
                k = len(range(i, SLOTS, QUAD))
                s0 = t * P + j * QS
                last = copy(prod[i * ROWS:(i + 1) * ROWS, 0:k, s0 + q0:s0 + q1],
                            picked[j * ROWS:(j + 1) * ROWS, t % 2, i:SLOTS:QUAD, q0:q1])
            return last

        def together(t):
            return [range(UNITS)] if t < LAST else [range(u, u + 1) for u in range(UNITS)]

        @block.gpsimd
        def _(pool):
            nc.gpsimd.memset(ident[:], 0.0).then_inc(ident_zero, 1)
            for c, numbers in rownr.items():
                nc.gpsimd.iota(numbers[:], pattern=[[1, c]], base=0, channel_multiplier=c).then_inc(rownr_ready, 1)
            nc.gpsimd.memset(one[:], 1.0).then_inc(one_ready, 1)
            pool.wait_ge(ident_zero, 1)
            nc.gpsimd.affine_select(out=ident[:], in_=ident[:], compare_op=ALU.not_equal, fill=1.0, base=0,
                                    pattern=[[-1, P]], channel_multiplier=1).then_inc(ident_ready, 1)
            pool.wait_ge(ids_in, 16)
            for t in range(TILES):
                for k, group in enumerate(GROUPS[t]):
                    if t >= 2:
                        before = max(n for n, g in enumerate(GROUPS[t - 2]) if g[0] <= group[-1])
                        pool.wait_ge(turn_done, pass_nr["turn", t - 2, before] + 1)
                    for f in group:
                        g = f - NFULL - 1
                        pool.indirect_dma_start(
                            out=rows[:, t % 2, g, :], out_offset=None, in_=gathered[g],
                            in_offset=bass.IndirectOffsetOnAxis(ap=ids_sb[:, t, g:g + 1], axis=0),
                        ).then_inc(rows_in[t][k], 16)

        @block.tensor
        def _(pe):
            def bank_free(n):
                if n >= TBANKS:
                    pe.wait_ge(feat_ready, n - TBANKS + 1)

            def turn(t, k):
                n = pass_nr["turn", t, k]
                pe.wait_ge(rows_in[t][k], 16 * len(GROUPS[t][k]))
                bank_free(n)
                for i, f in enumerate(GROUPS[t][k]):
                    last = nc.tensor.transpose(turned[:, n % TBANKS, i * P:(i + 1) * P],
                                               rows[:, t % 2, f - NFULL - 1, :], ident[:])
                last.then_inc(turn_done, 1)

            def look(e):
                n = pass_nr["look", e]
                bank_free(n)
                for part, ready in ((high, high_ready), (low, low_ready)):
                    pe.wait_ge(ready, e + 1)
                    for c in range(CH[e]):
                        if part is high and c == CH[e] - ACT_CHUNKS:
                            pe.wait_ge(onehot_ready_act, e + 1)
                        elif part is high and c < CH[e] - ACT_CHUNKS and c % DVE_CHUNKS == 0:
                            pe.wait_ge(onehot_ready, dve_builds(e) + c // DVE_CHUNKS + 1)
                        last = nc.tensor.matmul(turned[:, n % TBANKS, looked_samples(e)], part[0:LP[e], e % 2, c, :],
                                                onehot[0:LP[e], e % 2, c, looked_samples(e)],
                                                start=(part is high and c == 0),
                                                stop=(part is low and c == CH[e] - 1))
                last.then_inc(turn_done, 1)

            def products(t):
                needed = [("look", e) for e in range(NLOOK) if FROM[e] <= t]
                needed += [("turn", t, k) for k in range(len(GROUPS[t]))]
                pe.wait_ge(feat_ready, max(pass_nr[step] for step in needed) + 1)
                for u in range(UNITS):
                    n = t * UNITS + u
                    if n >= GBANKS:
                        pe.wait_ge(unit_picked, n - GBANKS + 1)
                    for q in range(QU):
                        for j in range(QUAD):
                            sample = feat[:, t * P + j * QS + u * QU + q, :]
                            last = nc.tensor.matmul(gram[j * ROWS:j * ROWS + C, n % GBANKS, q * C:(q + 1) * C],
                                                    sample, sample, start=True, stop=True,
                                                    tile_position=(0, j * ROWS))
                    last.then_inc(gram_done, 1)

            def dense(t, half):
                if t:
                    pe.wait_ge(h1_ready, M1 * (t - 1) + 2 * half + 2)
                if t == LAST and half == 1:
                    bank_free(len(passes))
                for m in (2 * half, 2 * half + 1):
                    nc.tensor.matmul(h1_tile(t, m), wd[:, m * P:(m + 1) * P], xT[:, t * P:(t + 1) * P],
                                     start=(m % 2 == 0 or (t == LAST and m == M1 - 1)), stop=False,
                                     skip_group_check=True)

            def layer1(t, half):
                samples = slice(t * P, (t + 1) * P)
                pe.wait_ge(prod_ready, t + 1)
                pe.wait_ge(prod_ready_dve, t + 1)
                for m in (2 * half, 2 * half + 1):
                    cols = slice(m * P, (m + 1) * P)
                    for k in range(KT):
                        K = ROWS * min(QUAD, SLOTS - QUAD * k)
                        last = nc.tensor.matmul(h1_tile(t, m), wp[0:K, k, cols], prod[0:K, k, samples],
                                                start=False, stop=(k == KT - 1), skip_group_check=True)
                    if m % 2 or (t == LAST and m == M1 - 2):
                        last.then_inc(h1_done, 1)

            def layer2(t):
                if t:
                    pe.wait_ge(y_ready, t)
                for m in range(M2):
                    for k in range(M1):
                        if m == 0:
                            pe.wait_ge(h1_ready, M1 * t + k + 1)
                        last = nc.tensor.matmul(h2_tile(t, m), w2s[:, k, m * P:(m + 1) * P],
                                                h1[:, k, :], start=(k == 0), stop=(k == M1 - 1))
                    if m == M2 - 1 or t == LAST:
                        last.then_inc(h2_done, 1)

            def layer3(t):
                for k in range(M2):
                    pe.wait_ge(h2_ready, M2 * t + (k + 1 if t == LAST else M2))
                    last = nc.tensor.matmul(h2p[0:1, 0:P], w3s[:, k:k + 1], h2[:, k, :],
                                            start=(k == 0), stop=(k == M2 - 1))
                last.then_inc(y_done, 1)

            pe.wait_ge(ident_ready, 1)
            for what, *at in order:
                if what == "turn":
                    turn(*at)
                elif what == "look":
                    look(*at)
                elif what == "products":
                    if at == [0]:
                        pe.wait_ge(dense_feat, 1)
                        pe.wait_ge(gram_zero, 1)
                    products(*at)
                elif what == "dense":
                    if at == [0, 0]:
                        pe.wait_ge(wd_ready, 1)
                    dense(*at)
                elif what == "layer1":
                    if at == [0, 0]:
                        pe.wait_ge(wp_in, 16 * KT)
                    layer1(*at)
                elif what == "layer2":
                    if at == [0]:
                        pe.wait_ge(w2_in, 16)
                        pe.wait_ge(small_in, 48)
                    layer2(*at)
                elif what == "layer3":
                    layer3(*at)

        @block.scalar
        def _(act):
            def round_table(e):
                act.wait_ge(tab_in[e], 16)
                if e >= 2:
                    act.wait_ge(turn_done, pass_nr["look", e - 2] + 1)
                nc.scalar.copy(high[0:LP[e], e % 2, 0:CH[e], :], tab[0:LP[e], e % 2, 0:CH[e], :]
                               ).then_inc(high_ready, 1)

            def build_onehot(e):
                act.wait_ge(idl_in[e], 16)
                if e >= 1:
                    act.wait_ge(onehot_ready_act, e)
                samples = looked_samples(e)
                for a in range(ACT_CHUNKS):
                    c = CH[e] - ACT_CHUNKS + a
                    last = nc.scalar.activation(distance[0:LP[e], a, samples], idl[0:LP[e], e % 3, samples],
                                                ACT.Square, bias=rownr_f[CH[e]][0:LP[e], c:c + 1], scale=-1.0)
                last.then_inc(distance_ready, 1)
                if e >= 2:
                    act.wait_ge(turn_done, pass_nr["look", e - 2] + 1)
                act.wait_ge(distance_ready, e + 1)
                nc.scalar.activation(onehot[0:LP[e], e % 2, CH[e] - ACT_CHUNKS:CH[e], samples],
                                     distance[0:LP[e], :, samples],
                                     ACT.Relu, bias=one[0:LP[e]], scale=-1.0).then_inc(onehot_ready_act, 1)

            def copy_turned(t, k):
                n, g, f0 = pass_nr["turn", t, k], len(GROUPS[t][k]), GROUPS[t][k][0]
                act.wait_ge(turn_done, n + 1)
                nc.scalar.copy(feat[:, t * P:(t + 1) * P, f0:f0 + g].rearrange("p s f -> p f s"),
                               turned[:, n % TBANKS, 0:g * P].rearrange("p (f s) -> p f s", s=P)
                               ).then_inc(feat_ready, 1)

            def copy_looked(e):
                n = pass_nr["look", e]
                act.wait_ge(turn_done, n + 1)
                nc.scalar.copy(feat[:, looked_samples(e), e + 1], turned[:, n % TBANKS, looked_samples(e)]
                               ).then_inc(feat_ready, 1)

            def spread_tile(t):
                for units, share in zip(together(t), DVE_SHARE[t]):
                    act.wait_ge(unit_picked, t * UNITS + units.stop)
                    last = spread(nc.scalar.copy, t, SPREAD[share:], units)
                last.then_inc(prod_ready, 1)

            def relu1(t, half):
                if t:
                    act.wait_ge(h2_done, t)
                for m in (2 * half, 2 * half + 1):
                    act.wait_ge(h1_done, 2 * t + half + 1 + (t == LAST and m == M1 - 1))
                    nc.scalar.activation(h1[:, m, :], h1_tile(t, m), ACT.Relu, bias=b1s[:, m:m + 1]
                                         ).then_inc(h1_ready, 1)

            def relu2(t):
                if t:
                    act.wait_ge(y_done, t)
                for m in range(M2):
                    act.wait_ge(h2_done, t + 1 + (m if t == LAST else 0))
                    nc.scalar.activation(h2[:, m, :], h2_tile(t, m), ACT.Relu, bias=b2s[:, m:m + 1]
                                         ).then_inc(h2_ready, 1)

            def copy_y(t):
                act.wait_ge(y_done, t + 1)
                nc.scalar.copy(y[:, t * P:(t + 1) * P], h2p[0:1, 0:P]).then_inc(y_ready, 1)

            act.wait_ge(rownr_ready, len(rownr))
            for c, numbers in rownr_f.items():
                nc.scalar.copy(numbers[:], rownr[c][:]).then_inc(rownr_f_ready, 1)
            act.wait_ge(rownr_f_ready, len(rownr_f))
            act.wait_ge(one_ready, 1)
            for what, *at in order:
                if what == "turn":
                    copy_turned(*at)
                elif what == "look":
                    copy_looked(*at)
                elif what == "build":
                    round_table(*at)
                    build_onehot(*at)
                elif what == "copy_dense":
                    act.wait_ge(x_in, 16)
                    nc.scalar.copy(feat[:, :, 0], xT[:]).then_inc(dense_feat, 1)
                elif what == "products":
                    spread_tile(*at)
                elif what == "layer1":
                    if at == [0, 0]:
                        act.wait_ge(small_in, 48)
                    relu1(*at)
                elif what == "layer2":
                    relu2(*at)
                elif what == "layer3":
                    copy_y(*at)

        @block.vector
        def _(dve):
            def build_onehot(e):
                dve.wait_ge(idl_in[e], 16)
                if e >= 2:
                    dve.wait_ge(turn_done, pass_nr["look", e - 2] + 1)
                samples = looked_samples(e)
                for c in range(0, CH[e] - ACT_CHUNKS, DVE_CHUNKS):
                    chunks = slice(c, min(c + DVE_CHUNKS, CH[e] - ACT_CHUNKS))
                    shape = [LP[e], chunks.stop - c, B - samples.start]
                    of_samples = idl[0:LP[e], e % 3, samples].rearrange("p (o s) -> p o s", o=1).to_broadcast(shape)
                    of_rows = rownr[CH[e]][0:LP[e], chunks].rearrange("p (c o) -> p c o", o=1).to_broadcast(shape)
                    nc.vector.tensor_tensor(onehot[0:LP[e], e % 2, chunks, samples], of_samples, of_rows,
                                            ALU.is_equal).then_inc(onehot_ready, 1)

            def split_table(e):
                used = (slice(0, LP[e]), e % 2, slice(0, CH[e]))
                dve.wait_ge(high_ready, e + 1)
                nc.vector.tensor_tensor(low[used], tab[used], high[used].bitcast(F32), ALU.subtract
                                        ).then_inc(low_ready, 1)

            def pick(t, u):
                n = t * UNITS + u
                if t >= 2 and u == 0:
                    dve.wait_ge(prod_ready, t - 1)
                    dve.wait_ge(prod_ready_dve, t - 1)
                dve.wait_ge(gram_done, n + 1)
                unit = gram[:, n % GBANKS, 0:QU * C].rearrange("p (q c) -> p c q", c=C)
                to = picked[:, t % 2, :, u * QU:(u + 1) * QU]
                nc.vector.tensor_copy(to, unit[:, SLOTS - 1:C, :]).then_inc(second_picked, 1)
                dve.wait_ge(second_picked, n + 1)
                mask = first[:].rearrange("p (c o) -> p c o", o=1).to_broadcast([P, SLOTS - 1, QU])
                nc.vector.copy_predicated(to[:, 0:SLOTS - 1, :], mask, unit[:, 0:SLOTS - 1, :]
                                          ).then_inc(unit_picked, 1)

            def pick_tile(t):
                for units, share in zip(together(t), DVE_SHARE[t]):
                    for u in units:
                        pick(t, u)
                    dve.wait_ge(unit_picked, t * UNITS + units.stop)
                    last = spread(nc.vector.tensor_copy, t, SPREAD[:share], units)
                last.then_inc(prod_ready_dve, 1)

            nc.vector.memset(gram[:], 0.0).then_inc(gram_zero, 1)
            dve.wait_ge(rownr_ready, len(rownr))
            for what, *at in order:
                if what == "build":
                    build_onehot(*at)
                    split_table(*at)
                elif what == "sum_dense":
                    dve.wait_ge(wd_in, 16)
                    nc.vector.tensor_tensor(wd, wd, wd2[:, 1, :], ALU.add).then_inc(wd_ready, 1)
                elif what == "products":
                    if at == [0]:
                        dve.wait_ge(first_in, 16)
                        dve.wait_ge(gram_zero, 1)
                    pick_tile(*at)


_LOOKED = [3, 6, 13, 17, 19, 25]
_LOOKED_LATE = [0, 1, 4, 7]
_PLACES = _LOOKED + _LOOKED_LATE + [f for f in range(26) if f not in _LOOKED + _LOOKED_LATE]


def kernel(**inputs):
    import numpy as _np
    import concourse.bacc as _bacc
    from concourse import mybir as _mybir
    from concourse.bass_utils import run_bass_kernel_spmd as _run

    x, ids, W1 = (_np.asarray(inputs[n]) for n in ("r_dense_features", "ids", "W_top1"))
    W2, W3 = inputs["W_top2"], inputs["W_top3"]
    B, D = x.shape
    F = ids.shape[1]
    NL = len(_LOOKED)
    H1, H2 = W2.shape
    place = [0] + [_PLACES.index(f) + 1 for f in range(F)]
    slots, first_rows = slots_of(F + 1)
    at, row = [], D
    for a in range(F):
        for b in range(a + 1, F + 1):
            c, r = place[a], place[b]
            if (r - c) % (F + 1) >= slots:
                c, r = r, c
            slot = c if c < slots - 1 else c - (slots - 1)
            at.append((ROWS * (slot % QUAD) + r, slot // QUAD))
            row += 1
    assert len(set(at)) == len(at)
    w_pairs = _np.zeros((P, -(-slots // QUAD), H1), W1.dtype)
    w_pairs[tuple(_np.array(at).T)] = W1[D:row]
    first = _np.zeros((QUAD, ROWS, slots - 1), _np.int32)
    for c, rows in enumerate(first_rows):
        first[:, list(rows), c] = 1
    laid_out = {
        "x_T": x.T,
        "ids": ids[:, _PLACES[NL:]].reshape(B // P, P, F - NL).transpose(1, 0, 2),
        "ids_looked": ids[:, _LOOKED + _LOOKED_LATE].T,
        **{f"tbl_{f}": inputs[f"tbl_{f}"] for f in range(F)},
        "first_column": first.reshape(P, slots - 1),
        "w_pairs": w_pairs,
        "w_dense": _np.stack([W1[:D], W1[row:]], axis=1),
        "b1": _np.asarray(inputs["b_top1"]).reshape(H1 // P, P).T,
        "w2": _np.asarray(W2).reshape(H1 // P, P, H2).transpose(1, 0, 2),
        "b2": _np.asarray(inputs["b_top2"]).reshape(H2 // P, P).T,
        "w3": _np.asarray(W3).reshape(H2 // P, P).T,
    }
    nc = _bacc.Bacc("TRN2", target_bir_lowering=False, num_devices=1)
    arrays, aps = {}, {}
    for name, a in laid_out.items():
        a = _np.ascontiguousarray(a)
        arrays[f"in_{name}"] = a
        aps[name] = nc.dram_tensor(f"in_{name}", a.shape, _mybir.dt.from_np(a.dtype), kind="ExternalInput").ap()
    out = nc.dram_tensor("out", (1, B), F32, kind="ExternalOutput").ap()
    tables = [aps[f"tbl_{f}"] for f in _PLACES]
    looked, gathered = tables[:NL + len(_LOOKED_LATE)], tables[NL:]
    interaction_tower(nc, aps["x_T"], aps["ids"], aps["ids_looked"], looked, gathered, F + 1,
                      aps["first_column"], aps["w_pairs"], aps["w_dense"], aps["b1"], aps["w2"], aps["b2"],
                      aps["w3"], out)
    r = _run(nc, [arrays], core_ids=[0])
    return r.results[0]["out"].reshape(B, 1)
```
